# Optimizing a Trainium2 kernel written in Bass

```python
import numpy as np
import jax
import jax.numpy as jnp

def _softmax(x, axis=-1):
    return jax.nn.softmax(x, axis=axis)

def _gelu(x):
    return jax.nn.gelu(x, approximate=True)

def _silu(x):
    return jax.nn.silu(x)

def _sigmoid(x):
    return jax.nn.sigmoid(x)

def _layernorm(x, axis=-1, eps=1e-05):
    m = jnp.mean(x, axis=axis, keepdims=True)
    v = jnp.var(x, axis=axis, keepdims=True)
    return (x - m) / jnp.sqrt(v + eps)

def _scatter_add(tgt, idx, src, axis=0):
    return tgt.at[idx].add(src)

def _segment_sum(src, seg, n):
    return jax.ops.segment_sum(src, seg, n)
kernel_name = 'mk_rec_standalone_d1_rec_r8_2b2dd8'

def setup_inputs(seed: int=0):
    np.random.seed(seed)
    _w = jnp.asarray

    def _rec_inputs():
        import jax
        import jax.numpy as jnp
        _rk = jax.random.key(seed)
        r_features = jax.random.uniform(jax.random.fold_in(_rk, 1), (1024, 2, 5128), jnp.float32, 0.0, 1)
        r_stm = 0.00782532 + 1.00527 * jax.random.normal(jax.random.fold_in(_rk, 2), (1024, 2, 1), jnp.float32)
        return (r_features, r_stm)
    r_features, r_stm = _rec_inputs()

    def _L0_rec_setup():
        import jax, jax.numpy as jnp
        import numpy as np
        B, P, NUM_FEATURES, M = (512, 2, 5128, 512)
        key = jax.random.key(seed)
        ks = jax.random.split(key, 8)
        return {'features': jax.random.uniform(ks[0], (B, P, NUM_FEATURES), dtype=jnp.float32), 'stm': jax.random.normal(ks[1], (B, P, 1), dtype=jnp.float32), 'W_ft': jax.random.normal(ks[2], (M, NUM_FEATURES), dtype=jnp.float32) * 0.01, 'b_ft': jax.random.normal(ks[3], (M,), dtype=jnp.float32) * 0.01, 'W1': jax.random.normal(ks[4], (32, 2 * M), dtype=jnp.float32) * 0.05, 'b1': jax.random.normal(ks[5], (32,), dtype=jnp.float32) * 0.05, 'W2': jax.random.normal(ks[6], (1, 32), dtype=jnp.float32) * 0.1, 'b2': jax.random.normal(ks[7], (1,), dtype=jnp.float32) * 0.1}
    _L0_rec_all = _L0_rec_setup()
    _L0_rec_in = {k: v for k, v in _L0_rec_all.items() if k in ('W_ft', 'b_ft', 'W1', 'b1', 'W2', 'b2')}
    del _L0_rec_all
    return {'r_features': r_features, 'r_stm': r_stm, 'L0_rec_W_ft': _L0_rec_in['W_ft'], 'L0_rec_b_ft': _L0_rec_in['b_ft'], 'L0_rec_W1': _L0_rec_in['W1'], 'L0_rec_b1': _L0_rec_in['b1'], 'L0_rec_W2': _L0_rec_in['W2'], 'L0_rec_b2': _L0_rec_in['b2']}

def reference(r_features, r_stm, L0_rec_W_ft, L0_rec_b_ft, L0_rec_W1, L0_rec_b1, L0_rec_W2, L0_rec_b2):
    import jax
    import jax.numpy as jnp

    def _L0_rec_ref(features, stm, W_ft, b_ft, W1, b1, W2, b2):
        import jax, jax.numpy as jnp
        import numpy as np
        B, P, NUM_FEATURES, M = (512, 2, 5128, 512)
        w = jnp.einsum('bpf,mf->bpm', features, W_ft) + b_ft
        accumulator = stm * w
        l1_x = jnp.clip(accumulator, 0.0, 1.0).reshape(features.shape[0], -1)
        l2_x = jnp.clip(l1_x @ W1.T + b1, 0.0, 1.0)
        return l2_x @ W2.T + b2
    y = _L0_rec_ref(r_features, r_stm, L0_rec_W_ft, L0_rec_b_ft, L0_rec_W1, L0_rec_b1, L0_rec_W2, L0_rec_b2)
    return y

_drawn_inputs = setup_inputs


def setup_inputs(seed=0):
    import zlib

    import numpy as np

    out = dict(_drawn_inputs(seed))
    spreads = {}
    factors = {'L0_rec_b_ft': 2.797}
    for name, (base, spread) in spreads.items():
        noise = np.random.default_rng([zlib.crc32(name.encode()), seed]).standard_normal(out[name].shape)
        drawn = base * np.exp(spread * noise) if base else spread * noise
        out[name] = jnp.asarray(drawn.astype(out[name].dtype))
    for name, factor in factors.items():
        out[name] = (out[name] * factor).astype(out[name].dtype)
    return out
```

```python
from contextlib import ExitStack

import concourse.bass as bass
from concourse import mybir

F32 = mybir.dt.float32
F32R = mybir.dt.float32r
ALU = mybir.AluOpType
ACT = mybir.ActivationFunctionType

P = 128
BANK = 512
SLOTS = 4


def feature_net(nc, x_t, w_t, stm, b_ft, w1_t, b1, w2_t, b2, out):
    HALVES, F, ROWS = x_t.shape
    M = w_t.shape[1]
    PERSP = ROWS // BANK
    UT = M // P
    STEPS = F // P
    REST = F - STEPS * P
    GROUPS = STEPS // SLOTS
    L1 = w1_t.shape[1]
    KT1 = PERSP * UT
    assert STEPS % SLOTS == 0 and GROUPS >= 3 and 0 < REST <= 32 and PERSP * UT == 8

    x_rows = x_t.rearrange("h f r -> (h f) r")

    ctx = ExitStack()
    with ctx:
        def sb(name, shape, dt=F32):
            return ctx.enter_context(nc.sbuf_tensor(name, shape, dt))

        def sem(name):
            return ctx.enter_context(nc.semaphore(name))

        x_raw = sb("x_raw", [P, SLOTS, ROWS])
        w_raw = sb("w_raw", [P, SLOTS, M])
        x_hi = sb("x_hi", [P, SLOTS, ROWS], F32R)
        x_lo = sb("x_lo", [P, SLOTS, ROWS], F32R)
        w_hi = sb("w_hi", [P, SLOTS, M], F32R)
        w_lo = sb("w_lo", [P, SLOTS, M], F32R)
        xr_raw = sb("xr_raw", [P, HALVES, ROWS])
        wr_raw = sb("wr_raw", [P, M])
        xr = sb("xr", [P, HALVES, ROWS], F32R)
        wr = sb("wr", [P, M], F32R)
        stm_all = sb("stm_all", [P, HALVES, PERSP, BANK])
        b_ft_col = sb("b_ft_col", [P, UT])
        act = sb("act", [P, HALVES, PERSP, UT, BANK])
        w1_sb = sb("w1_sb", [P, KT1, L1])
        b1_col = sb("b1_col", [L1, 1])
        w2_sb = sb("w2_sb", [L1, 1])
        b2_sb = sb("b2_sb", [1, 1])
        hid = sb("hid", [L1, HALVES, BANK])
        res = sb("res", [1, HALVES * BANK])
        sums = ctx.enter_context(nc.psum_tensor("sums", [P, UT, PERSP, BANK], F32))

        x_loaded = [sem(f"x_loaded{j}") for j in range(SLOTS)]
        w_loaded = [sem(f"w_loaded{j}") for j in range(SLOTS)]
        x_hi_ready = sem("x_hi_ready")
        w_hi_ready = sem("w_hi_ready")
        x_lo_ready = sem("x_lo_ready")
        w_lo_ready = sem("w_lo_ready")
        step_done = sem("step_done")
        sums_full = sem("sums_full")
        sums_free = sem("sums_free")
        act_ready = sem("act_ready")
        rest_zeroed = sem("rest_zeroed")
        rest_loaded = sem("rest_loaded")
        rest_hi = sem("rest_hi")
        rest_ready = sem("rest_ready")
        const_loaded = sem("const_loaded")
        head_loaded = sem("head_loaded")
        l1_full = sem("l1_full")
        l1_relu = sem("l1_relu")
        hid_ready = sem("hid_ready")
        l2_full = sem("l2_full")
        res_ready = sem("res_ready")
        stored = sem("stored")

        HEAD_DMAS = 4
        CONST_DMAS = 2

        def uses(step, j):
            return (step - j) * (16 // SLOTS) + 16

        def all_steps(eng, one_step):
            for half in range(HALVES):
                base = half * STEPS
                for j in range(SLOTS):
                    one_step(half, base, j, True, False)
                with eng.Fori(1, GROUPS - 1) as g:
                    for j in range(SLOTS):
                        one_step(half, base + g * SLOTS, j, False, False)
                for j in range(SLOTS):
                    one_step(half, base + STEPS - SLOTS, j, False, True)

        block = ctx.enter_context(nc.Block())

        @block.sync
        def _(sp):
            def load(half, s0, j, first, last):
                s = s0 + j
                reused = half > 0 or not first
                if reused:
                    sp.wait_ge(w_lo_ready, s - SLOTS + 1)
                sp.dma_start(w_raw[:, j, :], w_t[bass.ds((s - half * STEPS) * P, P), :])\
                    .then_inc(w_loaded[j], 16)
                if reused:
                    sp.wait_ge(x_lo_ready, s - SLOTS + 1)
                sp.dma_start(x_raw[:, j, :], x_rows[bass.ds(s * P + half * REST, P), :])\
                    .then_inc(x_loaded[j], 16)

            all_steps(sp, load)
            sp.wait_ge(res_ready, HALVES)
            sp.dma_start(out.rearrange("(a n) -> a n", a=1), res[:, :]).then_inc(stored, 16)
            sp.wait_ge(stored, 16)

        @block.gpsimd
        def _(pool):
            pool.memset(xr_raw[:, :, :], 0.0).then_inc(rest_zeroed, 1)
            pool.memset(wr_raw[:, :], 0.0).then_inc(rest_zeroed, 1)
            pool.wait_ge(x_loaded[1], 16)
            pool.wait_ge(rest_zeroed, 2)
            for q in range(0, P, 32):
                pool.dma_start(xr_raw[q:q + REST, :, :],
                               x_t[:, STEPS * P:F, :].rearrange("h f r -> f h r")).then_inc(rest_loaded, 16)
                pool.dma_start(wr_raw[q:q + REST, :], w_t[STEPS * P:F, :]).then_inc(rest_loaded, 16)
            pool.dma_start(stm_all[:, :, :, :].rearrange("p h c n -> p (h c n)"),
                           stm.rearrange("(a n) -> a n", a=1).broadcast_to([P, HALVES * ROWS]))\
                .then_inc(const_loaded, 16)
            pool.dma_start(b_ft_col[:, :], b_ft).then_inc(const_loaded, 16)
            pool.dma_start(w1_sb[:, :, :], w1_t.rearrange("(k p) o -> p k o", p=P)).then_inc(head_loaded, 16)
            pool.dma_start(b1_col[:, :], b1).then_inc(head_loaded, 16)
            pool.dma_start(w2_sb[:, :], w2_t).then_inc(head_loaded, 16)
            pool.dma_start(b2_sb[:, :], b2).then_inc(head_loaded, 16)

        @block.scalar
        def _(sc):
            def split_hi(half, s0, j, first, last):
                s = s0 + j
                if half > 0 or not first:
                    sc.wait_ge(step_done, s - SLOTS + 1)
                sc.wait_ge(w_loaded[j], uses(s, j))
                nc.scalar.activation(w_hi[:, j, :], w_raw[:, j, :], ACT.Copy).then_inc(w_hi_ready, 1)
                sc.wait_ge(x_loaded[j], uses(s, j))
                nc.scalar.activation(x_hi[:, j, :], x_raw[:, j, :], ACT.Copy).then_inc(x_hi_ready, 1)
                if half == 0 and first and j == SLOTS - 1:
                    sc.wait_ge(rest_loaded, 16 * 8)
                    nc.scalar.activation(xr[:, :, :], xr_raw[:, :, :], ACT.Copy).then_inc(rest_hi, 1)
                    nc.scalar.activation(wr[:, :], wr_raw[:, :], ACT.Copy).then_inc(rest_hi, 1)

            all_steps(sc, split_hi)

        @block.vector
        def _(dve):
            def drain(half):
                dve.wait_ge(const_loaded, 16 * CONST_DMAS)
                for m in range(UT):
                    n = half * UT + m + 1
                    if m < UT - 1:
                        dve.wait_ge(sums_full, half * (UT - 1) + m + 1)
                    else:
                        dve.wait_ge(step_done, (half + 1) * STEPS)
                    for c in range(PERSP):
                        out_of_banks = nc.vector.scalar_tensor_tensor(
                            out=act[:, half, c, m, :], in0=sums[:, m, c, :],
                            scalar=b_ft_col[:, m:m + 1], in1=stm_all[:, half, c, :],
                            op0=ALU.add, op1=ALU.mult)
                    out_of_banks.then_inc(sums_free, 1)
                    dve.wait_ge(sums_free, n)
                    nc.vector.tensor_scalar(act[:, half, :, m, :], act[:, half, :, m, :],
                                            0.0, 1.0, ALU.max, ALU.min).then_inc(act_ready, 1)

            def split_lo(half, s0, j, first, last):
                s = s0 + j
                if half > 0 and first and j == SLOTS - 1:
                    drain(half - 1)
                dve.wait_ge(w_hi_ready, s + 1)
                nc.vector.tensor_tensor(w_lo[:, j, :], w_raw[:, j, :], w_hi[:, j, :].bitcast(F32),
                                        ALU.subtract).then_inc(w_lo_ready, 1)
                dve.wait_ge(x_hi_ready, s + 1)
                nc.vector.tensor_tensor(x_lo[:, j, :], x_raw[:, j, :], x_hi[:, j, :].bitcast(F32),
                                        ALU.subtract).then_inc(x_lo_ready, 1)
                if half == 0 and first and j == SLOTS - 1:
                    dve.wait_ge(rest_hi, 2)
                    for q in (32, 96):
                        nc.vector.tensor_tensor(xr[q:q + 32, :, :], xr_raw[q:q + 32, :, :],
                                                xr[q:q + 32, :, :].bitcast(F32), ALU.subtract)\
                            .then_inc(rest_ready, 1)
                    nc.vector.tensor_tensor(wr[64:P, :], wr_raw[64:P, :], wr[64:P, :].bitcast(F32),
                                            ALU.subtract).then_inc(rest_ready, 1)

            all_steps(dve, split_lo)
            drain(HALVES - 1)
            dve.wait_ge(head_loaded, 16 * HEAD_DMAS)
            for h in range(HALVES):
                dve.wait_ge(l1_full, h + 1)
                nc.vector.tensor_scalar(hid[:, h, :], sums[0:L1, 0, h, :], b1_col[:, 0:1], 0.0,
                                        ALU.add, ALU.max).then_inc(l1_relu, 1)
                dve.wait_ge(l1_relu, h + 1)
                nc.vector.tensor_scalar(hid[:, h, :], hid[:, h, :], 1.0, None, ALU.min).then_inc(hid_ready, 1)
            for h in range(HALVES):
                dve.wait_ge(l2_full, h + 1)
                nc.vector.tensor_scalar(res[:, h * BANK:(h + 1) * BANK], sums[0:1, 1, h, :],
                                        b2_sb[:, 0:1], None, ALU.add).then_inc(res_ready, 1)

        @block.tensor
        def _(pe):
            def products(half, s0, j, first, last):
                s = s0 + j
                start = first and j == 0
                closing = last and j == SLOTS - 1
                if closing:
                    if half == 0:
                        pe.wait_ge(rest_ready, 3)
                    for m in range(UT):
                        for c in range(PERSP):
                            nc.tensor.matmul(sums[:, m, c, :], wr[:, m * P:(m + 1) * P],
                                             xr[:, half, c * BANK:(c + 1) * BANK], start=False, stop=False)
                pe.wait_ge(w_hi_ready, s + 1)
                pe.wait_ge(x_hi_ready, s + 1)
                for m in range(UT):
                    units = slice(m * P, (m + 1) * P)
                    if start and half > 0:
                        pe.wait_ge(sums_free, (half - 1) * UT + m + 1)
                    for c in range(PERSP):
                        nc.tensor.matmul(sums[:, m, c, :], w_hi[:, j, units],
                                         x_hi[:, j, c * BANK:(c + 1) * BANK], start=start, stop=False)
                    if m == 0:
                        pe.wait_ge(w_lo_ready, s + 1)
                        pe.wait_ge(x_lo_ready, s + 1)
                    for c in range(PERSP):
                        nc.tensor.matmul(sums[:, m, c, :], w_hi[:, j, units],
                                         x_lo[:, j, c * BANK:(c + 1) * BANK], start=False, stop=False)
                    for c in range(PERSP):
                        mm = nc.tensor.matmul(sums[:, m, c, :], w_lo[:, j, units],
                                              x_hi[:, j, c * BANK:(c + 1) * BANK], start=False, stop=closing)
                    if m == UT - 1:
                        mm.then_inc(step_done, 1)
                    elif closing:
                        mm.then_inc(sums_full, 1)

            all_steps(pe, products)

            pe.wait_ge(head_loaded, 16 * HEAD_DMAS)
            pe.wait_ge(sums_free, (HALVES - 1) * UT + 1)
            for h in range(HALVES):
                for m in range(UT):
                    pe.wait_ge(act_ready, h * UT + m + 1)
                    for c in range(PERSP):
                        mm = nc.tensor.matmul(sums[0:L1, 0, h, :], w1_sb[:, c * UT + m, :],
                                              act[:, h, c, m, :], start=(m == 0 and c == 0),
                                              stop=(m == UT - 1 and c == PERSP - 1))
                mm.then_inc(l1_full, 1)
            for h in range(HALVES):
                pe.wait_ge(hid_ready, h + 1)
                nc.tensor.matmul(sums[0:1, 1, h, :], w2_sb[:, :], hid[:, h, :], start=True, stop=True)\
                    .then_inc(l2_full, 1)


def kernel(**inputs):
    import numpy as np
    import concourse.bacc as bacc
    from concourse.bass_utils import run_bass_kernel_spmd

    arr = {k: np.asarray(v) for k, v in inputs.items()}
    x = arr["r_features"]
    B, PERSP, F = x.shape
    HALVES = 2
    half = B // HALVES
    x_t = np.ascontiguousarray(x.reshape(HALVES, half, PERSP, F).transpose(0, 3, 2, 1))
    laid_out = {
        "x_t": x_t.reshape(HALVES, F, PERSP * half),
        "w_t": np.ascontiguousarray(arr["L0_rec_W_ft"].T),
        "stm": np.ascontiguousarray(
            arr["r_stm"].reshape(HALVES, half, PERSP).transpose(0, 2, 1)).reshape(-1),
        "b_ft": np.ascontiguousarray(arr["L0_rec_b_ft"].reshape(-1, 128).T),
        "w1_t": np.ascontiguousarray(arr["L0_rec_W1"].T),
        "b1": arr["L0_rec_b1"].reshape(-1, 1),
        "w2_t": np.ascontiguousarray(arr["L0_rec_W2"].T),
        "b2": arr["L0_rec_b2"].reshape(1, 1),
    }
    nc = bacc.Bacc("TRN2", target_bir_lowering=False, num_devices=1)
    args = [nc.dram_tensor(k, a.shape, mybir.dt.from_np(a.dtype), kind="ExternalInput").ap()
            for k, a in laid_out.items()]
    out = nc.dram_tensor("out", (B,), F32, kind="ExternalOutput").ap()
    feature_net(nc, *args, out)
    r = run_bass_kernel_spmd(nc, [laid_out], core_ids=[0])
    return r.results[0]["out"].reshape(B, 1)
```

```python
from contextlib import ExitStack

import concourse.bass as bass
from concourse import mybir

F32 = mybir.dt.float32
F32R = mybir.dt.float32r
ALU = mybir.AluOpType
ACT = mybir.ActivationFunctionType

P = 128
BANK = 512
SLOTS = 4
WARM_UP = 8


def feature_net(nc, x_t, w_t, stm, b_ft, w1_t, b1, w2_t, b2, out):
    HALVES, F, ROWS = x_t.shape
    M = w_t.shape[1]
    PERSP = ROWS // BANK
    UT = M // P
    BANKS = UT * PERSP
    STEPS = F // P
    REST = F - STEPS * P
    GROUPS = STEPS // SLOTS
    L1 = w1_t.shape[1]
    KT1 = BANKS
    Q = P // L1
    QB = BANK // Q
    assert STEPS % SLOTS == 0 and GROUPS >= 3 and 0 < REST <= L1 == 32 and BANKS == 8

    x_rows = x_t.rearrange("h f r -> (h f) r")

    ctx = ExitStack()
    with ctx:
        def sb(name, shape, dt=F32):
            return ctx.enter_context(nc.sbuf_tensor(name, shape, dt))

        def sem(name):
            return ctx.enter_context(nc.semaphore(name))

        x_raw = sb("x_raw", [P, SLOTS, ROWS])
        w_raw = sb("w_raw", [P, SLOTS, M])
        x_hi = sb("x_hi", [P, SLOTS, ROWS], F32R)
        x_lo = sb("x_lo", [P, SLOTS, ROWS], F32R)
        w_hi = sb("w_hi", [P, SLOTS, M], F32R)
        w_lo = sb("w_lo", [P, SLOTS, M], F32R)
        xr_raw = sb("xr_raw", [P, HALVES, ROWS])
        wr_raw = sb("wr_raw", [P, M])
        xr = sb("xr", [P, HALVES, ROWS], F32R)
        wr = sb("wr", [P, M], F32R)
        stm_all = sb("stm_all", [P, HALVES, PERSP, BANK])
        b_ft_col = sb("b_ft_col", [P, UT])
        act = sb("act", [P, HALVES, PERSP, UT, BANK])
        w1_sb = sb("w1_sb", [P, KT1, L1])
        b1_col = sb("b1_col", [P, 1])
        add_up = sb("add_up", [P, L1])
        part = sb("part", [P, HALVES, BANK])
        idle = sb("idle", [P, BANK], mybir.dt.bfloat16)
        w2_diag = sb("w2_diag", [P, Q])
        b2_col = sb("b2_col", [Q, 1])
        hid = sb("hid", [P, HALVES, QB])
        res = sb("res", [Q, HALVES, QB])
        sums = ctx.enter_context(nc.psum_tensor("sums", [P, UT, PERSP, BANK], F32))

        x_loaded = [sem(f"x_loaded{j}") for j in range(SLOTS)]
        w_loaded = [sem(f"w_loaded{j}") for j in range(SLOTS)]
        x_hi_ready = sem("x_hi_ready")
        w_hi_ready = sem("w_hi_ready")
        x_lo_ready = sem("x_lo_ready")
        w_lo_ready = sem("w_lo_ready")
        step_done = sem("step_done")
        bank_full = sem("bank_full")
        bank_free = sem("bank_free")
        act_ready = sem("act_ready")
        idle_zeroed = sem("idle_zeroed")
        first_loaded = [sem(f"first_loaded{n}") for n in range(4)]
        first_hi = sem("first_hi")
        first_lo = sem("first_lo")
        add_up_built = sem("add_up_built")
        padded = sem("padded")
        rest_loaded = sem("rest_loaded")
        rest_hi = sem("rest_hi")
        rest_ready = sem("rest_ready")
        const_loaded = sem("const_loaded")
        head_loaded = sem("head_loaded")
        l1_full = sem("l1_full")
        part_ready = sem("part_ready")
        l1_summed = sem("l1_summed")
        hid_ready = sem("hid_ready")
        l2_full = sem("l2_full")
        res_ready = sem("res_ready")
        stored = sem("stored")

        REST_DMAS = 2 * P // 32
        CONST_DMAS = 2
        HEAD_DMAS = 2 + 2 * Q

        def uses(step, j):
            return (step - j) * (16 // SLOTS) + (16 if j > 0 else 0)

        def all_steps(eng, one_step):
            for half in range(HALVES):
                base = half * STEPS
                for j in range(SLOTS):
                    one_step(half, base, j, True, False)
                with eng.Fori(1, GROUPS - 1) as g:
                    for j in range(SLOTS):
                        one_step(half, base + g * SLOTS, j, False, False)
                for j in range(SLOTS):
                    one_step(half, base + STEPS - SLOTS, j, False, True)

        block = ctx.enter_context(nc.Block())

        @block.sync
        def _(sp):
            sp.dma_start(w_raw[:, 0, 0:P], w_t[0:P, 0:P]).then_inc(first_loaded[0], 16)
            for c in range(PERSP):
                sp.dma_start(x_raw[:, 0, c * BANK:(c + 1) * BANK],
                             x_rows[0:P, c * BANK:(c + 1) * BANK]).then_inc(first_loaded[1 + c], 16)
            sp.dma_start(w_raw[:, 0, P:M], w_t[0:P, P:M]).then_inc(first_loaded[3], 16)

            def load(half, s0, j, first, last):
                s = s0 + j
                if half == 0 and first and j == 0:
                    return
                reused = half > 0 or not first
                if reused:
                    sp.wait_ge(w_lo_ready, s - SLOTS + 1)
                sp.dma_start(w_raw[:, j, :], w_t[bass.ds((s - half * STEPS) * P, P), :])\
                    .then_inc(w_loaded[j], 16)
                if reused:
                    sp.wait_ge(x_lo_ready, s - SLOTS + 1)
                sp.dma_start(x_raw[:, j, :], x_rows[bass.ds(s * P + half * REST, P), :])\
                    .then_inc(x_loaded[j], 16)

            all_steps(sp, load)
            sp.wait_ge(res_ready, HALVES)
            sp.dma_start(out.rearrange("(h q n) -> q h n", h=HALVES, q=Q), res[:, :, :])\
                .then_inc(stored, 16)
            sp.wait_ge(stored, 16)

        @block.gpsimd
        def _(pool):
            pool.memset(add_up[:, :], 0.0).then_inc(add_up_built, 1)
            pool.memset(b1_col[:, :], 0.0).then_inc(padded, 1)
            pool.memset(w2_diag[:, :], 0.0).then_inc(padded, 1)
            for g in range(P // L1):
                pool.wait_ge(add_up_built, g + 1)
                pool.affine_select(out=add_up[:, :], in_=add_up[:, :], compare_op=ALU.not_equal, fill=1.0,
                                   base=-L1 * g, pattern=[[-1, L1]], channel_multiplier=1)\
                    .then_inc(add_up_built, 1)
            pool.memset(xr_raw[:, :, :], 0.0).then_inc(padded, 1)
            pool.memset(wr_raw[:, :], 0.0).then_inc(padded, 1)
            pool.wait_ge(x_loaded[1], 16)
            pool.wait_ge(padded, 4)
            for q in range(0, P, 32):
                pool.dma_start(xr_raw[q:q + REST, :, :],
                               x_t[:, STEPS * P:F, :].rearrange("h f r -> f h r")).then_inc(rest_loaded, 16)
                pool.dma_start(wr_raw[q:q + REST, :], w_t[STEPS * P:F, :]).then_inc(rest_loaded, 16)
            pool.dma_start(stm_all[:, :, :, :].rearrange("p h c n -> p (h c n)"),
                           stm.rearrange("(a n) -> a n", a=1).broadcast_to([P, HALVES * ROWS]))\
                .then_inc(const_loaded, 16)
            pool.dma_start(b_ft_col[:, :], b_ft).then_inc(const_loaded, 16)
            pool.dma_start(w1_sb[:, :, :], w1_t.rearrange("(k p) o -> p k o", p=P)).then_inc(head_loaded, 16)
            pool.dma_start(b1_col[0:L1, :], b1).then_inc(head_loaded, 16)
            for q in range(Q):
                pool.dma_start(w2_diag[q * L1:(q + 1) * L1, q:q + 1], w2_t).then_inc(head_loaded, 16)
                pool.dma_start(b2_col[q:q + 1, :], b2).then_inc(head_loaded, 16)

        @block.scalar
        def _(sc):
            def split_hi(half, s0, j, first, last):
                s = s0 + j
                if half == 0 and first and j == 0:
                    sc.wait_ge(first_loaded[0], 16)
                    nc.scalar.activation(w_hi[:, 0, 0:P], w_raw[:, 0, 0:P], ACT.Copy).then_inc(first_hi, 1)
                    sc.wait_ge(first_loaded[1], 16)
                    nc.scalar.activation(x_hi[:, 0, 0:BANK], x_raw[:, 0, 0:BANK], ACT.Copy)\
                        .then_inc(first_hi, 1)
                    sc.wait_ge(first_loaded[2], 16)
                    nc.scalar.activation(x_hi[:, 0, BANK:ROWS], x_raw[:, 0, BANK:ROWS], ACT.Copy)\
                        .then_inc(x_hi_ready, 1)
                    sc.wait_ge(first_loaded[3], 16)
                    nc.scalar.activation(w_hi[:, 0, P:M], w_raw[:, 0, P:M], ACT.Copy).then_inc(w_hi_ready, 1)
                    return
                if half > 0 or not first:
                    sc.wait_ge(step_done, s - SLOTS + 1)
                sc.wait_ge(w_loaded[j], uses(s, j))
                nc.scalar.activation(w_hi[:, j, :], w_raw[:, j, :], ACT.Copy).then_inc(w_hi_ready, 1)
                sc.wait_ge(x_loaded[j], uses(s, j))
                nc.scalar.activation(x_hi[:, j, :], x_raw[:, j, :], ACT.Copy).then_inc(x_hi_ready, 1)
                if half == 0 and last and j == 0:
                    sc.wait_ge(rest_loaded, 16 * REST_DMAS)
                    nc.scalar.activation(xr[:, :, :], xr_raw[:, :, :], ACT.Copy).then_inc(rest_hi, 1)
                    nc.scalar.activation(wr[:, :], wr_raw[:, :], ACT.Copy).then_inc(rest_hi, 1)

            all_steps(sc, split_hi)
            sc.wait_ge(head_loaded, 16 * HEAD_DMAS)
            for h in range(HALVES):
                sc.wait_ge(l1_full, h + 1)
                nc.scalar.activation(part[:, h, :], sums[:, 0, h, :], ACT.Identity,
                                     bias=b1_col[:, 0:1]).then_inc(part_ready, 1)

        @block.vector
        def _(dve):
            def drain(half):
                dve.wait_ge(const_loaded, 16 * CONST_DMAS)
                for bank in range(BANKS):
                    m, c = divmod(bank, PERSP)
                    n = half * BANKS + bank + 1
                    if bank < BANKS - 1:
                        dve.wait_ge(bank_full, n - half)
                    else:
                        dve.wait_ge(step_done, (half + 1) * STEPS)
                    nc.vector.scalar_tensor_tensor(
                        out=act[:, half, c, m, :], in0=sums[:, m, c, :], scalar=b_ft_col[:, m:m + 1],
                        in1=stm_all[:, half, c, :], op0=ALU.add, op1=ALU.mult).then_inc(bank_free, 1)
                    dve.wait_ge(bank_free, n)
                    nc.vector.tensor_scalar(act[:, half, c, m, :], act[:, half, c, m, :],
                                            0.0, 1.0, ALU.max, ALU.min).then_inc(act_ready, 1)

            def split_lo(half, s0, j, first, last):
                s = s0 + j
                if half > 0 and first and j == SLOTS - 2:
                    drain(half - 1)
                if half == 0 and first and j == 0:
                    dve.wait_ge(first_hi, 1)
                    nc.vector.tensor_tensor(w_lo[:, 0, 0:P], w_raw[:, 0, 0:P], w_hi[:, 0, 0:P].bitcast(F32),
                                            ALU.subtract).then_inc(first_lo, 1)
                    dve.wait_ge(first_hi, 2)
                    nc.vector.tensor_tensor(x_lo[:, 0, 0:BANK], x_raw[:, 0, 0:BANK],
                                            x_hi[:, 0, 0:BANK].bitcast(F32), ALU.subtract)\
                        .then_inc(first_lo, 1)
                    dve.wait_ge(x_hi_ready, 1)
                    nc.vector.tensor_tensor(x_lo[:, 0, BANK:ROWS], x_raw[:, 0, BANK:ROWS],
                                            x_hi[:, 0, BANK:ROWS].bitcast(F32), ALU.subtract)\
                        .then_inc(x_lo_ready, 1)
                    dve.wait_ge(w_hi_ready, 1)
                    nc.vector.tensor_tensor(w_lo[:, 0, P:M], w_raw[:, 0, P:M], w_hi[:, 0, P:M].bitcast(F32),
                                            ALU.subtract).then_inc(w_lo_ready, 1)
                    return
                dve.wait_ge(w_hi_ready, s + 1)
                nc.vector.tensor_tensor(w_lo[:, j, :], w_raw[:, j, :], w_hi[:, j, :].bitcast(F32),
                                        ALU.subtract).then_inc(w_lo_ready, 1)
                dve.wait_ge(x_hi_ready, s + 1)
                nc.vector.tensor_tensor(x_lo[:, j, :], x_raw[:, j, :], x_hi[:, j, :].bitcast(F32),
                                        ALU.subtract).then_inc(x_lo_ready, 1)
                if half == 0 and last and j == 0:
                    dve.wait_ge(rest_hi, 2)
                    for q in (32, 96):
                        nc.vector.tensor_tensor(xr[q:q + 32, :, :], xr_raw[q:q + 32, :, :],
                                                xr[q:q + 32, :, :].bitcast(F32), ALU.subtract)\
                            .then_inc(rest_ready, 1)
                    nc.vector.tensor_tensor(wr[64:P, :], wr_raw[64:P, :], wr[64:P, :].bitcast(F32),
                                            ALU.subtract).then_inc(rest_ready, 1)

            nc.vector.memset(idle[:, :], 0.0).then_inc(idle_zeroed, 1)
            all_steps(dve, split_lo)
            drain(HALVES - 1)
            dve.wait_ge(head_loaded, 16 * HEAD_DMAS)
            for h in range(HALVES):
                dve.wait_ge(l1_summed, h + 1)
                nc.vector.tensor_scalar(hid[:, h, :], sums[:, 1, h, 0:QB], 0.0, 1.0,
                                        ALU.max, ALU.min).then_inc(hid_ready, 1)
            for h in range(HALVES):
                dve.wait_ge(l2_full, h + 1)
                nc.vector.tensor_scalar(res[:, h, :], sums[0:Q, 2, h, 0:QB],
                                        b2_col[:, 0:1], None, ALU.add).then_inc(res_ready, 1)

        @block.tensor
        def _(pe):
            def product(m, c, w, x, j, **flags):
                return nc.tensor.matmul(sums[:, m, c, :], w[:, j, m * P:(m + 1) * P],
                                        x[:, j, c * BANK:(c + 1) * BANK], **flags)

            def opening():
                for m in range(UT):
                    if m == 1:
                        pe.wait_ge(w_hi_ready, 1)
                    for c in range(PERSP):
                        if m == 0 and c == 0:
                            pe.wait_ge(first_hi, 2)
                        elif m == 0:
                            pe.wait_ge(x_hi_ready, 1)
                        product(m, c, w_hi, x_hi, 0, start=True, stop=False)
                    if m == 0:
                        pe.wait_ge(first_lo, 2)
                        product(m, 0, w_hi, x_lo, 0, start=False, stop=False)
                    if m == 1:
                        pe.wait_ge(w_lo_ready, 1)
                    for c in range(PERSP):
                        product(m, c, w_lo, x_hi, 0, start=False, stop=False)
                    if m == 0:
                        pe.wait_ge(x_lo_ready, 1)
                    for c in range(1 if m == 0 else 0, PERSP):
                        mm = product(m, c, w_hi, x_lo, 0, start=False, stop=False)
                mm.then_inc(step_done, 1)

            def closing(half, s):
                if half == 0:
                    pe.wait_ge(rest_ready, 3)
                for parts in (w_hi_ready, x_hi_ready, w_lo_ready, x_lo_ready):
                    pe.wait_ge(parts, s + 1)
                for m in range(UT):
                    for c in range(PERSP):
                        nc.tensor.matmul(sums[:, m, c, :], wr[:, m * P:(m + 1) * P],
                                         xr[:, half, c * BANK:(c + 1) * BANK], start=False, stop=False)
                        for j in (SLOTS - 2, SLOTS - 1):
                            end = j == SLOTS - 1
                            product(m, c, w_hi, x_hi, j, start=False, stop=False)
                            product(m, c, w_hi, x_lo, j, start=False, stop=False)
                            mm = product(m, c, w_lo, x_hi, j, start=False, stop=end)
                            if m == UT - 1 and c == PERSP - 1:
                                mm.then_inc(step_done, 1)
                            elif end:
                                mm.then_inc(bank_full, 1)

            def products(half, s0, j, first, last):
                s = s0 + j
                if half == 0 and first and j == 0:
                    return opening()
                if last and j >= SLOTS - 2:
                    return closing(half, s) if j == SLOTS - 1 else None
                start = first and j == 0
                pe.wait_ge(w_hi_ready, s + 1)
                pe.wait_ge(x_hi_ready, s + 1)
                for m in range(UT):
                    for c in range(PERSP):
                        if start:
                            pe.wait_ge(bank_free, (half - 1) * BANKS + m * PERSP + c + 1)
                        product(m, c, w_hi, x_hi, j, start=start, stop=False)
                    if m == 0:
                        pe.wait_ge(w_lo_ready, s + 1)
                        pe.wait_ge(x_lo_ready, s + 1)
                    for c in range(PERSP):
                        product(m, c, w_hi, x_lo, j, start=False, stop=False)
                    for c in range(PERSP):
                        mm = product(m, c, w_lo, x_hi, j, start=False, stop=False)
                mm.then_inc(step_done, 1)

            pe.wait_ge(idle_zeroed, 1)
            for _ in range(WARM_UP):
                nc.tensor.matmul(sums[:, UT - 1, PERSP - 1, :], idle[:, 0:P], idle[:, :],
                                 start=True, stop=True)
            all_steps(pe, products)

            pe.wait_ge(head_loaded, 16 * HEAD_DMAS)
            pe.wait_ge(bank_free, (HALVES - 1) * BANKS + PERSP)
            for h in range(HALVES):
                for m in range(UT):
                    for c in range(PERSP):
                        pe.wait_ge(act_ready, h * BANKS + m * PERSP + c + 1)
                        q = (c * 2 + m % 2) * L1
                        mm = nc.tensor.matmul(sums[q:q + L1, 0, h, :], w1_sb[:, c * UT + m, :],
                                              act[:, h, c, m, :], start=m < 2, stop=m >= UT - 2)
                mm.then_inc(l1_full, 1)
            pe.wait_ge(add_up_built, 1 + Q)
            for h in range(HALVES):
                pe.wait_ge(part_ready, h + 1)
                for q in range(Q):
                    mm = nc.tensor.matmul(sums[q * L1:(q + 1) * L1, 1, h, 0:QB], add_up[:, :],
                                          part[:, h, q * QB:(q + 1) * QB], start=True, stop=True)
                mm.then_inc(l1_summed, 1)
            for h in range(HALVES):
                pe.wait_ge(hid_ready, h + 1)
                nc.tensor.matmul(sums[0:Q, 2, h, 0:QB], w2_diag[:, :], hid[:, h, :],
                                 start=True, stop=True).then_inc(l2_full, 1)


def kernel(**inputs):
    import numpy as np
    import concourse.bacc as bacc
    from concourse.bass_utils import run_bass_kernel_spmd

    arr = {k: np.asarray(v) for k, v in inputs.items()}
    x = arr["r_features"]
    B, PERSP, F = x.shape
    HALVES = 2
    half = B // HALVES
    x_t = np.ascontiguousarray(x.reshape(HALVES, half, PERSP, F).transpose(0, 3, 2, 1))
    laid_out = {
        "x_t": x_t.reshape(HALVES, F, PERSP * half),
        "w_t": np.ascontiguousarray(arr["L0_rec_W_ft"].T),
        "stm": np.ascontiguousarray(
            arr["r_stm"].reshape(HALVES, half, PERSP).transpose(0, 2, 1)).reshape(-1),
        "b_ft": np.ascontiguousarray(arr["L0_rec_b_ft"].reshape(-1, 128).T),
        "w1_t": np.ascontiguousarray(arr["L0_rec_W1"].T),
        "b1": arr["L0_rec_b1"].reshape(-1, 1),
        "w2_t": np.ascontiguousarray(arr["L0_rec_W2"].T),
        "b2": arr["L0_rec_b2"].reshape(1, 1),
    }
    nc = bacc.Bacc("TRN2", target_bir_lowering=False, num_devices=1)
    args = [nc.dram_tensor(k, a.shape, mybir.dt.from_np(a.dtype), kind="ExternalInput").ap()
            for k, a in laid_out.items()]
    out = nc.dram_tensor("out", (B,), F32, kind="ExternalOutput").ap()
    feature_net(nc, *args, out)
    r = run_bass_kernel_spmd(nc, [laid_out], core_ids=[0])
    return r.results[0]["out"].reshape(B, 1)
```
